# Optimizing a Trainium2 kernel written in Bass

```python
import numpy as np
import jax
import jax.numpy as jnp

def _softmax(x, axis=-1):
    return jax.nn.softmax(x, axis=axis)

def _gelu(x):
    return jax.nn.gelu(x, approximate=True)

def _silu(x):
    return jax.nn.silu(x)

def _sigmoid(x):
    return jax.nn.sigmoid(x)

def _layernorm(x, axis=-1, eps=1e-05):
    m = jnp.mean(x, axis=axis, keepdims=True)
    v = jnp.var(x, axis=axis, keepdims=True)
    return (x - m) / jnp.sqrt(v + eps)

def _scatter_add(tgt, idx, src, axis=0):
    return tgt.at[idx].add(src)

def _segment_sum(src, seg, n):
    return jax.ops.segment_sum(src, seg, n)
kernel_name = 'mk_recurrent_d2_jaxref_r8_1f1211'

def setup_inputs(seed: int=0):
    np.random.seed(seed)
    _w = jnp.asarray

    def _L0_attn_setup():
        import jax, jax.numpy as jnp
        import numpy as np
        DIM = 128
        HEADS = 16
        HEAD_DIM = 64
        key = jax.random.key(seed)
        ks = jax.random.split(key, 6)
        inner = HEADS * HEAD_DIM
        s = 0.02
        return {'x': jax.random.normal(ks[0], (2, 256, DIM), dtype=jnp.float32), 'Wq': jax.random.normal(ks[1], (DIM, inner), dtype=jnp.float32) * s, 'Wk': jax.random.normal(ks[2], (DIM, inner), dtype=jnp.float32) * s, 'Wv': jax.random.normal(ks[3], (DIM, inner), dtype=jnp.float32) * s, 'Wo': jax.random.normal(ks[4], (inner, DIM), dtype=jnp.float32) * s, 'bo': jax.random.normal(ks[5], (DIM,), dtype=jnp.float32) * s}
    _L0_attn_in = _L0_attn_setup()

    def _L0_ffn_setup():
        import jax, jax.numpy as jnp
        import numpy as np
        B, S, D, E, F, K = (4, 128, 128, 8, 352, 1)
        key = jax.random.key(seed)
        ks = jax.random.split(key, 8)
        sc = 0.02
        return {'x_bsD': jax.random.normal(ks[0], (B, S, D), jnp.float32), 'router_DE': jax.random.normal(ks[1], (D, E), jnp.float32) * sc, 'w1_eDF': jax.random.normal(ks[2], (E, D, F), jnp.float32) * sc, 'w3_eDF': jax.random.normal(ks[3], (E, D, F), jnp.float32) * sc, 'w2_eFD': jax.random.normal(ks[4], (E, F, D), jnp.float32) * sc, 'ws1_DF': jax.random.normal(ks[5], (D, F), jnp.float32) * sc, 'ws3_DF': jax.random.normal(ks[6], (D, F), jnp.float32) * sc, 'ws2_FD': jax.random.normal(ks[7], (F, D), jnp.float32) * sc}
    _L0_ffn_in = _L0_ffn_setup()

    def _L1_attn_setup():
        import jax, jax.numpy as jnp
        import numpy as np
        EPS = 1e-06
        NUM_HEADS = 16

        def _phi(x):
            return jax.nn.elu(x) + 1.0
        key = jax.random.key(seed)
        ks = jax.random.split(key, 5)
        B, S, D = (2, 256, 128)
        scale = 1.0 / np.sqrt(D)
        return {'x': jax.random.normal(ks[0], (B, S, D), dtype=jnp.float32), 'Wq': jax.random.normal(ks[1], (D, D), dtype=jnp.float32) * scale, 'bq': jnp.zeros((D,), dtype=jnp.float32), 'Wk': jax.random.normal(ks[2], (D, D), dtype=jnp.float32) * scale, 'bk': jnp.zeros((D,), dtype=jnp.float32), 'Wv': jax.random.normal(ks[3], (D, D), dtype=jnp.float32) * scale, 'bv': jnp.zeros((D,), dtype=jnp.float32), 'Wo': jax.random.normal(ks[4], (D, D), dtype=jnp.float32) * scale, 'bo': jnp.zeros((D,), dtype=jnp.float32)}
    _L1_attn_in = _L1_attn_setup()

    def _L1_ffn_setup():
        import jax, jax.numpy as jnp
        import numpy as np
        DIM = 128
        DEPTH = 2
        HEADS = 8
        DIM_HEAD = 64
        WINDOW = 64
        INNER = HEADS * DIM_HEAD
        HID = int(DIM * 4 * 2 / 3)
        B, N = (2, 1024)
        QK_SCALE = 8.0

        def shift_token(t):
            t1, t2 = jnp.split(t, 2, axis=-1)
            t2 = jnp.pad(t2, ((0, 0), (1, 0), (0, 0)))[:, :-1]
            return jnp.concatenate([t1, t2], axis=-1)

        def l2norm(t):
            return t / jnp.clip(jnp.linalg.norm(t, axis=-1, keepdims=True), 1e-12)

        def rotate_half(x):
            x1, x2 = jnp.split(x, 2, axis=-1)
            return jnp.concatenate([-x2, x1], axis=-1)

        def rotary_xpos(q, k):
            n = q.shape[-2]
            half_idx = jnp.arange(0, DIM_HEAD, 2, dtype=jnp.float32)
            inv_freq = 1.0 / 10000.0 ** (half_idx / DIM_HEAD)
            t = jnp.arange(n, dtype=jnp.float32)
            freqs = t[:, None] * inv_freq[None, :]
            freqs = jnp.concatenate([freqs, freqs], axis=-1)
            base = (half_idx + 0.4 * DIM_HEAD) / (1.4 * DIM_HEAD)
            power = (t - n // 2) / float(WINDOW // 2)
            scale = base[None, :] ** power[:, None]
            scale = jnp.concatenate([scale, scale], axis=-1)
            cos, sin = (jnp.cos(freqs), jnp.sin(freqs))
            q = q * cos * scale + rotate_half(q) * sin * scale
            k = k * cos / scale + rotate_half(k) * sin / scale
            return (q, k)

        def local_attention(q, k, v):
            b, h, n, d = q.shape
            w = n // WINDOW
            bq = q.reshape(b, h, w, WINDOW, d) * QK_SCALE
            bk = k.reshape(b, h, w, WINDOW, d)
            bv = v.reshape(b, h, w, WINDOW, d)

            def look_around(t):
                p = jnp.pad(t, ((0, 0), (0, 0), (1, 0), (0, 0), (0, 0)))
                return jnp.concatenate([p[:, :, :w], p[:, :, 1:]], axis=3)
            bk, bv = (look_around(bk), look_around(bv))
            bt = jnp.arange(n).reshape(w, WINDOW)
            btp = jnp.pad(bt, ((1, 0), (0, 0)), constant_values=-1)
            btk = jnp.concatenate([btp[:w], btp[1:]], axis=1)
            sim = jnp.einsum('bhwid,bhwjd->bhwij', bq, bk)
            i = bt[:, :, None]
            j = btk[:, None, :]
            mask = (i < j) | (i > j + WINDOW) | (j == -1)
            sim = jnp.where(mask, -jnp.finfo(sim.dtype).max, sim)
            attn = jax.nn.softmax(sim, axis=-1)
            out = jnp.einsum('bhwij,bhwjd->bhwid', attn, bv)
            return out.reshape(b, h, n, d)

        def _layer(x, wqkv, qs, ksc, wo, lg, lb, w1, b1, w2, b2):
            b, n, _ = x.shape
            h = shift_token(x)
            qkv = h @ wqkv
            q, k, v = jnp.split(qkv, 3, axis=-1)
            to_heads = lambda t: t.reshape(b, n, HEADS, DIM_HEAD).transpose(0, 2, 1, 3)
            q, k, v = (to_heads(q), to_heads(k), to_heads(v))
            q = l2norm(q) * qs
            k = l2norm(k) * ksc
            q, k = rotary_xpos(q, k)
            o = local_attention(q, k, v)
            o = o.transpose(0, 2, 1, 3).reshape(b, n, INNER)
            x = x + o @ wo
            h = shift_token(x)
            mu = h.mean(-1, keepdims=True)
            var = h.var(-1, keepdims=True)
            h = (h - mu) / jnp.sqrt(var + 1e-05) * lg + lb
            h = h @ w1 + b1
            a, g = jnp.split(h, 2, axis=-1)
            h = a * jax.nn.gelu(g, approximate=False)
            x = x + h @ w2 + b2
            return x
        key = jax.random.key(seed)
        ks = jax.random.split(key, 6)
        return {'x': jax.random.normal(ks[0], (B, N, DIM), jnp.float32), 'wqkv': jax.random.normal(ks[1], (DEPTH, DIM, 3 * INNER), jnp.float32) * 0.02, 'q_scale': jnp.ones((DEPTH, DIM_HEAD), jnp.float32), 'k_scale': jnp.ones((DEPTH, DIM_HEAD), jnp.float32), 'wo': jax.random.normal(ks[2], (DEPTH, INNER, DIM), jnp.float32) * 0.02, 'ln_g': jnp.ones((DEPTH, DIM), jnp.float32), 'ln_b': jnp.zeros((DEPTH, DIM), jnp.float32), 'w1': jax.random.normal(ks[3], (DEPTH, DIM, 2 * HID), jnp.float32) * 0.02, 'b1': jnp.zeros((DEPTH, 2 * HID), jnp.float32), 'w2': jax.random.normal(ks[4], (DEPTH, HID, DIM), jnp.float32) * 0.02, 'b2': jnp.zeros((DEPTH, DIM), jnp.float32)}
    _L1_ffn_in = _L1_ffn_setup()
    _d = {'L0_attn_x': _L0_attn_in['x'], 'L0_attn_Wq': _L0_attn_in['Wq'], 'L0_attn_Wk': _L0_attn_in['Wk'], 'L0_attn_Wv': _L0_attn_in['Wv'], 'L0_attn_Wo': _L0_attn_in['Wo'], 'L0_attn_bo': _L0_attn_in['bo'], 'L0_ffn_router_DE': _L0_ffn_in['router_DE'], 'L0_ffn_w1_eDF': _L0_ffn_in['w1_eDF'], 'L0_ffn_w3_eDF': _L0_ffn_in['w3_eDF'], 'L0_ffn_w2_eFD': _L0_ffn_in['w2_eFD'], 'L0_ffn_ws1_DF': _L0_ffn_in['ws1_DF'], 'L0_ffn_ws3_DF': _L0_ffn_in['ws3_DF'], 'L0_ffn_ws2_FD': _L0_ffn_in['ws2_FD'], 'L1_attn_Wq': _L1_attn_in['Wq'], 'L1_attn_bq': _L1_attn_in['bq'], 'L1_attn_Wk': _L1_attn_in['Wk'], 'L1_attn_bk': _L1_attn_in['bk'], 'L1_attn_Wv': _L1_attn_in['Wv'], 'L1_attn_bv': _L1_attn_in['bv'], 'L1_attn_Wo': _L1_attn_in['Wo'], 'L1_attn_bo': _L1_attn_in['bo'], 'L1_ffn_wqkv': _L1_ffn_in['wqkv'], 'L1_ffn_q_scale': _L1_ffn_in['q_scale'], 'L1_ffn_k_scale': _L1_ffn_in['k_scale'], 'L1_ffn_wo': _L1_ffn_in['wo'], 'L1_ffn_ln_g': _L1_ffn_in['ln_g'], 'L1_ffn_ln_b': _L1_ffn_in['ln_b'], 'L1_ffn_w1': _L1_ffn_in['w1'], 'L1_ffn_b1': _L1_ffn_in['b1'], 'L1_ffn_w2': _L1_ffn_in['w2'], 'L1_ffn_b2': _L1_ffn_in['b2']}
    _x0 = _d['L0_attn_x']
    _d['L0_attn_x'] = jax.random.normal(jax.random.fold_in(jax.random.key(seed), 1), (16, 256, 128), dtype=_x0.dtype)
    del _x0
    return _d

def reference(L0_attn_x, L0_attn_Wq, L0_attn_Wk, L0_attn_Wv, L0_attn_Wo, L0_attn_bo, L0_ffn_router_DE, L0_ffn_w1_eDF, L0_ffn_w3_eDF, L0_ffn_w2_eFD, L0_ffn_ws1_DF, L0_ffn_ws3_DF, L0_ffn_ws2_FD, L1_attn_Wq, L1_attn_bq, L1_attn_Wk, L1_attn_bk, L1_attn_Wv, L1_attn_bv, L1_attn_Wo, L1_attn_bo, L1_ffn_wqkv, L1_ffn_q_scale, L1_ffn_k_scale, L1_ffn_wo, L1_ffn_ln_g, L1_ffn_ln_b, L1_ffn_w1, L1_ffn_b1, L1_ffn_w2, L1_ffn_b2):

    def _L0_attn_ref(x, Wq, Wk, Wv, Wo, bo):
        import jax, jax.numpy as jnp
        import numpy as np
        DIM = 128
        HEADS = 16
        HEAD_DIM = 64
        N, S, _ = x.shape
        scale = 1.0 / np.sqrt(HEAD_DIM).astype(np.float32)
        q = (x @ Wq).reshape(N, S, HEADS, HEAD_DIM).transpose(0, 2, 1, 3)
        k = (x @ Wk).reshape(N, S, HEADS, HEAD_DIM).transpose(0, 2, 1, 3)
        v = (x @ Wv).reshape(N, S, HEADS, HEAD_DIM).transpose(0, 2, 1, 3)
        logits = jnp.einsum('nhid,nhjd->nhij', q, k) * scale
        causal = 1000000000.0 * (jnp.tril(jnp.ones((S, S), dtype=logits.dtype)) - 1.0)
        logits = logits + causal[None, None, :, :]
        attn = jax.nn.softmax(logits, axis=-1)
        out = jnp.einsum('nhij,nhjd->nhid', attn, v)
        out = out.transpose(0, 2, 1, 3).reshape(N, S, HEADS * HEAD_DIM)
        return out @ Wo + bo

    def _L0_ffn_ref(x_bsD, router_DE, w1_eDF, w3_eDF, w2_eFD, ws1_DF, ws3_DF, ws2_FD):
        import jax, jax.numpy as jnp
        import numpy as np
        B, S, D, E, F, K = (4, 128, 128, 8, 352, 1)
        b, s, d = x_bsD.shape
        a = b * s
        x_aD = x_bsD.reshape(a, d)
        scores_aE = x_aD @ router_DE
        vals_aK, idx_aK = jax.lax.top_k(scores_aE, K)
        masked_aE = jnp.full_like(scores_aE, -jnp.inf).at[jnp.arange(a)[:, None], idx_aK].set(vals_aK)
        gates_Ea = jax.nn.sigmoid(masked_aE).T
        routed_in_EaD = jax.lax.stop_gradient(gates_Ea[:, :, None] * x_aD[None, :, :])
        mid_EaF = jax.nn.silu(jnp.einsum('ead,edf->eaf', routed_in_EaD, w1_eDF)) * jnp.einsum('ead,edf->eaf', routed_in_EaD, w3_eDF)
        routed_out_EaD = jnp.einsum('eaf,efd->ead', mid_EaF, w2_eFD)
        shared_aD = jax.nn.silu(x_aD @ ws1_DF) * (x_aD @ ws3_DF) @ ws2_FD
        out_aD = shared_aD + routed_out_EaD.sum(axis=0)
        return out_aD.reshape(b, s, d)

    def _L1_attn_ref(x, Wq, bq, Wk, bk, Wv, bv, Wo, bo):
        import jax, jax.numpy as jnp
        import numpy as np
        EPS = 1e-06
        NUM_HEADS = 16

        def _phi(x):
            return jax.nn.elu(x) + 1.0
        B, S, D = x.shape
        H = NUM_HEADS
        hd = D // H
        q = (x @ Wq.T + bq).reshape(B, S, H, hd).transpose(0, 2, 1, 3)
        k = (x @ Wk.T + bk).reshape(B, S, H, hd).transpose(0, 2, 1, 3)
        v = (x @ Wv.T + bv).reshape(B, S, H, hd).transpose(0, 2, 1, 3)
        q = _phi(q)
        k = _phi(k)
        kv_cum = jnp.cumsum(k[..., :, None] * v[..., None, :], axis=2)
        k_cum = jnp.cumsum(k, axis=2)
        num = jnp.einsum('bhsd,bhsde->bhse', q, kv_cum)
        den = jnp.einsum('bhsd,bhsd->bhs', q, k_cum)
        out = num / (den[..., None] + EPS)
        out = out.transpose(0, 2, 1, 3).reshape(B, S, D)
        return out @ Wo.T + bo

    def _L1_ffn_ref(x, wqkv, q_scale, k_scale, wo, ln_g, ln_b, w1, b1, w2, b2):
        import jax, jax.numpy as jnp
        import numpy as np
        DIM = 128
        DEPTH = 2
        HEADS = 8
        DIM_HEAD = 64
        WINDOW = 64
        INNER = HEADS * DIM_HEAD
        HID = int(DIM * 4 * 2 / 3)
        B, N = (2, 1024)
        QK_SCALE = 8.0

        def shift_token(t):
            t1, t2 = jnp.split(t, 2, axis=-1)
            t2 = jnp.pad(t2, ((0, 0), (1, 0), (0, 0)))[:, :-1]
            return jnp.concatenate([t1, t2], axis=-1)

        def l2norm(t):
            return t / jnp.clip(jnp.linalg.norm(t, axis=-1, keepdims=True), 1e-12)

        def rotate_half(x):
            x1, x2 = jnp.split(x, 2, axis=-1)
            return jnp.concatenate([-x2, x1], axis=-1)

        def rotary_xpos(q, k):
            n = q.shape[-2]
            half_idx = jnp.arange(0, DIM_HEAD, 2, dtype=jnp.float32)
            inv_freq = 1.0 / 10000.0 ** (half_idx / DIM_HEAD)
            t = jnp.arange(n, dtype=jnp.float32)
            freqs = t[:, None] * inv_freq[None, :]
            freqs = jnp.concatenate([freqs, freqs], axis=-1)
            base = (half_idx + 0.4 * DIM_HEAD) / (1.4 * DIM_HEAD)
            power = (t - n // 2) / float(WINDOW // 2)
            scale = base[None, :] ** power[:, None]
            scale = jnp.concatenate([scale, scale], axis=-1)
            cos, sin = (jnp.cos(freqs), jnp.sin(freqs))
            q = q * cos * scale + rotate_half(q) * sin * scale
            k = k * cos / scale + rotate_half(k) * sin / scale
            return (q, k)

        def local_attention(q, k, v):
            b, h, n, d = q.shape
            w = n // WINDOW
            bq = q.reshape(b, h, w, WINDOW, d) * QK_SCALE
            bk = k.reshape(b, h, w, WINDOW, d)
            bv = v.reshape(b, h, w, WINDOW, d)

            def look_around(t):
                p = jnp.pad(t, ((0, 0), (0, 0), (1, 0), (0, 0), (0, 0)))
                return jnp.concatenate([p[:, :, :w], p[:, :, 1:]], axis=3)
            bk, bv = (look_around(bk), look_around(bv))
            bt = jnp.arange(n).reshape(w, WINDOW)
            btp = jnp.pad(bt, ((1, 0), (0, 0)), constant_values=-1)
            btk = jnp.concatenate([btp[:w], btp[1:]], axis=1)
            sim = jnp.einsum('bhwid,bhwjd->bhwij', bq, bk)
            i = bt[:, :, None]
            j = btk[:, None, :]
            mask = (i < j) | (i > j + WINDOW) | (j == -1)
            sim = jnp.where(mask, -jnp.finfo(sim.dtype).max, sim)
            attn = jax.nn.softmax(sim, axis=-1)
            out = jnp.einsum('bhwij,bhwjd->bhwid', attn, bv)
            return out.reshape(b, h, n, d)

        def _layer(x, wqkv, qs, ksc, wo, lg, lb, w1, b1, w2, b2):
            b, n, _ = x.shape
            h = shift_token(x)
            qkv = h @ wqkv
            q, k, v = jnp.split(qkv, 3, axis=-1)
            to_heads = lambda t: t.reshape(b, n, HEADS, DIM_HEAD).transpose(0, 2, 1, 3)
            q, k, v = (to_heads(q), to_heads(k), to_heads(v))
            q = l2norm(q) * qs
            k = l2norm(k) * ksc
            q, k = rotary_xpos(q, k)
            o = local_attention(q, k, v)
            o = o.transpose(0, 2, 1, 3).reshape(b, n, INNER)
            x = x + o @ wo
            h = shift_token(x)
            mu = h.mean(-1, keepdims=True)
            var = h.var(-1, keepdims=True)
            h = (h - mu) / jnp.sqrt(var + 1e-05) * lg + lb
            h = h @ w1 + b1
            a, g = jnp.split(h, 2, axis=-1)
            h = a * jax.nn.gelu(g, approximate=False)
            x = x + h @ w2 + b2
            return x
        for l in range(DEPTH):
            x = _layer(x, wqkv[l], q_scale[l], k_scale[l], wo[l], ln_g[l], ln_b[l], w1[l], b1[l], w2[l], b2[l])
        return x
    x = L0_attn_x
    xn = _layernorm(x, axis=-1)
    s = _L0_attn_ref(xn, L0_attn_Wq, L0_attn_Wk, L0_attn_Wv, L0_attn_Wo, L0_attn_bo)
    g = _silu(_L0_ffn_ref(xn, L0_ffn_router_DE, L0_ffn_w1_eDF, L0_ffn_w3_eDF, L0_ffn_w2_eFD, L0_ffn_ws1_DF, L0_ffn_ws3_DF, L0_ffn_ws2_FD))
    x = x + s * g
    xn = _layernorm(x, axis=-1)
    s = _L1_attn_ref(xn, L1_attn_Wq, L1_attn_bq, L1_attn_Wk, L1_attn_bk, L1_attn_Wv, L1_attn_bv, L1_attn_Wo, L1_attn_bo)
    g = _silu(_L1_ffn_ref(xn, L1_ffn_wqkv, L1_ffn_q_scale, L1_ffn_k_scale, L1_ffn_wo, L1_ffn_ln_g, L1_ffn_ln_b, L1_ffn_w1, L1_ffn_b1, L1_ffn_w2, L1_ffn_b2))
    x = x + s * g
    return x

_drawn_inputs = setup_inputs


def setup_inputs(seed=0):
    import zlib

    import numpy as np

    out = dict(_drawn_inputs(seed))
    spreads = {'L1_attn_bq': (0.0, 2.0),
     'L1_attn_bk': (0.0, 2.0),
     'L1_attn_bv': (0.0, 0.1),
     'L1_attn_bo': (0.0, 0.1),
     'L1_ffn_q_scale': (1.0, 0.6),
     'L1_ffn_k_scale': (1.0, 0.6),
     'L1_ffn_ln_g': (1.0, 0.6),
     'L1_ffn_ln_b': (0.0, 0.8),
     'L1_ffn_b1': (0.0, 0.8),
     'L1_ffn_b2': (0.0, 2.0)}
    factors = {'L0_attn_Wq': 8.0,
     'L0_attn_Wk': 8.0,
     'L0_attn_Wv': 8.0,
     'L0_attn_Wo': 8.0,
     'L0_attn_bo': 8.0,
     'L0_ffn_router_DE': 8.0,
     'L0_ffn_w1_eDF': 8.0,
     'L0_ffn_w3_eDF': 8.0,
     'L0_ffn_w2_eFD': 8.0,
     'L0_ffn_ws1_DF': 8.0,
     'L0_ffn_ws3_DF': 8.0,
     'L0_ffn_ws2_FD': 8.0,
     'L1_attn_Wq': 3.859,
     'L1_ffn_wqkv': 7.452,
     'L1_ffn_wo': 7.658,
     'L1_ffn_w1': 8.0,
     'L1_ffn_w2': 8.0}
    for name, (base, spread) in spreads.items():
        noise = np.random.default_rng([zlib.crc32(name.encode()), seed]).standard_normal(out[name].shape)
        drawn = base * np.exp(spread * noise) if base else spread * noise
        out[name] = jnp.asarray(drawn.astype(out[name].dtype))
    for name, factor in factors.items():
        out[name] = (out[name] * factor).astype(out[name].dtype)
    return out
```

```python
import concourse.bass as bass
from concourse import mybir
from contextlib import ExitStack

FP32 = mybir.dt.float32
INT32 = mybir.dt.int32
ALU = mybir.AluOpType
ACT = mybir.ActivationFunctionType
AX = mybir.AxisListType

P = 128
TILES = 4
SEQ = 256
NSEQ = 16
LOOPS = NSEQ * SEQ // (TILES * P)
TOK = TILES * P
HD = 64
HEADS0, PAIRS0 = 16, 8
HEADS1, PAIRS1 = 8, 4
INNER1 = HEADS1 * HD
EXPERTS, FF = 8, 352
FCHUNKS = [(0, 128), (128, 128), (256, 96)]
GLU = 341
GCHUNK = 114
GCHUNKS = [(0, 114), (114, 114), (228, 113)]
LH, LD = 16, 8
LE = LD + 1
LCHUNKS = [(0, 6), (6, 5), (11, 5)]
LAYERS = 2
SB = 384
RB = 4
RSQRT_MAGIC = 1597463007.0


class Ring:

    def __init__(self, full, done, units, depth, it):
        self.full_sem, self.done_sem = full, done
        self.units, self.depth, self.it, self.k = units, depth, it, 0

    def take(self):
        k = self.k
        self.k += 1
        return k

    def full(self, k):
        return self.it * self.units + (k + 1)

    def free(self, k):
        return self.it * self.units + (max(k - self.depth + 1, 0) + 1)

    def done(self, k):
        return self.it * self.units + (k + 2)

    def close(self):
        assert self.k == self.units, (self.k, self.units)


class Chain:

    def __init__(self, eng, sem, steps, it):
        self.eng, self.sem, self.steps, self.it, self.k = eng, sem, steps, it, 0

    def __call__(self, ins):
        self.k += 1
        ins.then_inc(self.sem, 1)
        self.eng.wait_ge(self.sem, self.it * self.steps + self.k)

    def close(self):
        assert self.k == self.steps, (self.k, self.steps)


def newton_rsqrt(nc, link, r, v, scratch):
    link(nc.vector.tensor_scalar(scratch.bitcast(INT32), v.bitcast(INT32), 1, None, ALU.logical_shift_right))
    link(nc.vector.tensor_scalar(r.bitcast(INT32), scratch.bitcast(INT32), -1.0, RSQRT_MAGIC, ALU.mult, ALU.add))
    for _ in range(3):
        link(nc.vector.scalar_tensor_tensor(out=scratch, in0=r, scalar=-0.5, in1=r, op0=ALU.mult, op1=ALU.mult))
        link(nc.vector.tensor_tensor(scratch, scratch, v, ALU.mult))
        link(nc.vector.scalar_tensor_tensor(out=r, in0=scratch, scalar=1.5, in1=r, op0=ALU.add, op1=ALU.mult))


NEWTON = 11


def layernorm(nc, c, link, out_of, in_of, stats, mv, rstd, scratch):
    for t in range(TILES):
        last = nc.vector.bn_stats(stats[:, t, :], in_of(t))
    link(last)
    nc.vector.sem_inc(c.settled, 1)
    for t in range(TILES):
        last = nc.vector.bn_aggr(mv[:, t, :], stats[:, t, :])
    link(last)
    link(nc.vector.tensor_scalar(scratch[:, 0, 0:TILES], mv[:, :, 1], 1e-5, None, ALU.add))
    newton_rsqrt(nc, link, rstd[:, 0:TILES], scratch[:, 0, 0:TILES], scratch[:, 1, 0:TILES])
    for t in range(TILES):
        last = nc.vector.tensor_scalar(out_of(t), in_of(t), mv[:, t, 0:1], rstd[:, t:t + 1], ALU.subtract, ALU.mult)
    return last


LAYERNORM = 3 + NEWTON


class Buffers:

    def __init__(self, q, k, v, p, sm, pt, nmax, den, rden, o, mask, settled, ident, s_ps, pt_ps, o_ps):
        self.q, self.k, self.v = q, k, v
        self.sm, self.p, self.pt = sm, p, pt
        self.nmax, self.den, self.rden, self.o = nmax, den, rden, o
        self.mask, self.ident, self.settled = mask, ident, settled
        self.s_ps, self.pt_ps, self.o_ps = s_ps, pt_ps, o_ps


class Signals:

    def __init__(self, exp_done, pv_done):
        self.exp_done, self.pv_done = exp_done, pv_done


class Common:
    pass


class Attention:

    def __init__(self, nc, pairs, mem, sem):
        self.nc, self.pairs, self.m, self.s = nc, pairs, mem, sem
        self.units = pairs * 4

    def unit(self, u):
        return u // 4, (u // 2) % 2, u % 2

    def tensor(self, pe, it, r, produce, merge, base, extra=None):
        nc, m = self.nc, self.m
        produce(0, 0)
        produce(1, 0)
        for u in range(self.units + 5):
            pair, seq, h = self.unit(u)
            if u < self.units:
                if u % 4 == 0 and pair + 1 < self.pairs:
                    produce(0, pair + 1)
                if u % 4 == 2 and pair + 1 < self.pairs:
                    produce(1, pair + 1)
                if u % 4 == 0:
                    pe.wait_ge(r["mm"].done_sem, r["qk_done"][pair])
                k = r["s"].take()
                pe.wait_ge(r["s"].done_sem, r["s"].free(k))
                o, c = HD * h, SEQ * seq
                q = m.q[o:o + HD, pair % 2, c:c + SEQ]
                kk = m.k[o:o + HD, pair % 2, c:c + SEQ]
                nc.tensor.matmul(m.s_ps[k % 2][:, 0:P], q[:, 0:P], kk[:, 0:P], start=True, stop=True)
                nc.tensor.matmul(m.s_ps[k % 2][:, P:SB], q[:, P:SEQ], kk, start=True, stop=True)\
                    .then_inc(r["s"].full_sem, 1)
                if extra:
                    extra(u)
            v = u - 2
            if 0 <= v < self.units:
                k = r["pt"].take()
                pe.wait_ge(self.s.exp_done, r["exp"].full(base + v))
                pe.wait_ge(r["pt"].done_sem, r["pt"].free(k))
                for j in range(3):
                    last = nc.tensor.transpose(m.pt_ps[k % 2][:, j * P:(j + 1) * P],
                                               m.p[:, v % RB, j * P:(j + 1) * P], m.ident[:, :])
                last.then_inc(r["pt"].full_sem, 1)
                r["pt_of"][v] = k
            v = u - 3
            if 0 <= v < self.units:
                pair, seq, h = self.unit(v)
                if v % 4 == 0:
                    r["o_k"] = r["o"].take()
                    pe.wait_ge(r["o"].done_sem, r["o"].free(r["o_k"]))
                pe.wait_ge(r["pt"].done_sem, r["pt"].done(r["pt_of"][v]))
                o_ps = m.o_ps[r["o_k"] % 2]
                c = pair * P + h * HD
                t = 2 * seq
                o = lambda tile: o_ps[:, tile * P + h * HD:tile * P + (h + 1) * HD]
                pt = m.pt[:, v % 2, :]
                nc.tensor.matmul(o(t), pt[:, 0:P], m.v[:, t, c:c + HD], start=True, stop=True)
                nc.tensor.matmul(o(t + 1), pt[:, P:2 * P], m.v[:, t, c:c + HD], start=True, stop=False)
                last = nc.tensor.matmul(o(t + 1), pt[:, 2 * P:SB], m.v[:, t + 1, c:c + HD], start=False, stop=True)
                last.then_inc(self.s.pv_done, 1)
                if v % 4 == 3:
                    r["o_of"][pair] = r["o_k"]
            if u >= 8 and u % 4 == 0:
                pair = u // 4 - 2
                pe.wait_ge(r["o"].done_sem, r["o"].done(r["o_of"][pair]))
                merge(pair)

    def scalar(self, act, it, r, produce, merge, base, extra=None):
        nc, m = self.nc, self.m
        produce(0, 0)
        produce(1, 0)
        for u in range(self.units + 5):
            if u < self.units:
                pair = u // 4
                if u % 4 == 0 and pair + 1 < self.pairs:
                    produce(0, pair + 1)
                if u % 4 == 2 and pair + 1 < self.pairs:
                    produce(1, pair + 1)
                k = r["s"].take()
                act.wait_ge(r["s"].done_sem, r["s"].done(k))
                if u >= RB:
                    act.wait_ge(r["pt"].full_sem, r["pt"].full(r["pt"].take()))
                den = m.den[:, pair % 2, u % 4, :]
                nc.scalar.activation(m.p[:, u % RB, 0:P], m.sm[:, u % RB, 0:P], ACT.Exp,
                                     bias=m.nmax[:, u % RB, 0:1], scale=-1.0, accum_out=den[:, 0:1])
                nc.scalar.activation(m.p[:, u % RB, P:SB], m.sm[:, u % RB, P:SB], ACT.Exp,
                                     bias=m.nmax[:, u % RB, 1:2], scale=-1.0, accum_out=den[:, 1:2])\
                    .then_inc(self.s.exp_done, 1)
                if extra:
                    extra(u)
            if u >= 8 and u % 4 == 0:
                merge(u // 4 - 2)
        r["pt"].k += RB

    def vector(self, dve, it, r, scale_of, base, extra=None):
        nc, m = self.nc, self.m
        for u in range(self.units + 4):
            if u < self.units:
                pair, seq, h = self.unit(u)
                k = r["s"].take()
                dve.wait_ge(r["s"].full_sem, r["s"].full(k))
                if u >= RB:
                    dve.wait_ge(self.s.exp_done, r["exp"].full(base + u - RB))
                dve.sem_inc(m.settled, 1)
                for i, (a, b) in enumerate(((0, P), (P, SB))):
                    last = nc.vector.tensor_tensor_reduce(
                        out=m.sm[:, u % RB, a:b], in0=m.s_ps[k % 2][:, a:b], in1=m.mask[:, a:b],
                        scale=scale_of(seq, pair, h, i), scalar=3e38, op0=ALU.add, op1=ALU.min,
                        accum_out=m.nmax[:, u % RB, i:i + 1])
                    if i == 1:
                        last.then_inc(r["s"].done_sem, 1)
                if extra:
                    extra(u)
            v = u - 2
            if 0 <= v < self.units:
                k = r["pt"].take()
                dve.wait_ge(r["pt"].full_sem, r["pt"].full(k))
                if v >= 2:
                    dve.wait_ge(self.s.pv_done, r["exp"].full(base + v - 2))
                nc.vector.tensor_copy(m.pt[:, v % 2, :], m.pt_ps[k % 2][:, 0:SB]).then_inc(r["pt"].done_sem, 1)
            v = u - 3
            if 0 <= v < self.units and v % 4 == 3:
                pair = v // 4
                k = r["o"].take()
                dve.wait_ge(self.s.pv_done, r["exp"].full(base + v))
                r["link"](nc.vector.reciprocal(m.rden[:, :], m.den[:, pair % 2, :, :].rearrange("p u i -> p (u i)")))
                if pair >= 2:
                    dve.wait_ge(r["mm"].full_sem, r["merged"](pair - 2))
                rd = m.rden[:, :].rearrange("p (s h i) -> p s h i", s=2, h=2)
                for s in range(2):
                    out = m.o[:, pair % 2, 2 * s:2 * s + 2, :].rearrange("p t (h d) -> p t h d", h=2)
                    src = m.o_ps[k % 2][:, 2 * s * P:(2 * s + 2) * P].rearrange("p (t h d) -> p t h d", t=2, h=2)
                    w = rd[:, s, :, :].rearrange("p h t -> p t h").unsqueeze(3).to_broadcast([P, 2, 2, HD])
                    last = nc.vector.tensor_tensor(out, src, w, ALU.mult)
                last.then_inc(r["o"].done_sem, 1)


def attention_order(pairs):
    order = [("q", 0), ("k", 0)]
    for u in range(4 * pairs + 5):
        if u < 4 * pairs and u // 4 + 1 < pairs:
            order += [("q", u // 4 + 1)] if u % 4 == 0 else [("k", u // 4 + 1)] if u % 4 == 2 else []
        if u >= 8 and u % 4 == 0:
            order.append(("merge", u // 4 - 2))
    return order


QKV1 = 3 * INNER1


def pass1_operands(nc, ctx):
    def sb(name, shape):
        return ctx.enter_context(nc.sbuf_tensor(name, shape, FP32))

    c1 = Common()
    c1.lw = sb("lw", [P, 3, P])
    c1.lwo = sb("lwo", [P, P])
    c1.lb = sb("lb", [P, 3, P])
    c1.lbo = sb("lbo", [P, P])
    c1.wqkv = sb("wqkv", [P, LAYERS, QKV1])
    c1.wo = sb("fwo", [P, LAYERS, PAIRS1, P])
    c1.g1 = sb("g1", [P, LAYERS, 2 * GLU])
    c1.g2 = sb("g2", [P, LAYERS, 3, P])
    c1.gb1 = sb("gb1", [P, LAYERS, 2, 3])
    c1.gb2 = sb("gb2", [P, LAYERS, P])
    c1.ln = sb("ln", [P, 2, LAYERS])
    c1.tri = sb("tri", [P, 4, P])
    c1.rot = sb("rot", [P, 2, 2, 2, HD])
    c1.qks = sb("qks", [P, 2, LAYERS, HD])
    c1.loaded = ctx.enter_context(nc.semaphore("w1_loaded"))
    return c1


def load_pass1(sp, c1, w):
    loads = []

    def load(dst, src):
        sp.dma_start(dst, src).then_inc(c1.loaded, 16)
        loads.append(1)

    load(c1.tri[:, :, :], w["c_tri"])
    load(c1.rot[:, :, :, :, :], w["c_rot"])
    for i, (a, b) in enumerate(((w["lWq"], w["lbq"]), (w["lWk"], w["lbk"]), (w["lWv"], w["lbv"]))):
        load(c1.lw[:, i, :], a)
        load(c1.lb[:, i, :], b.partition_broadcast(P))
    load(c1.lwo[:, :], w["lWo"])
    load(c1.lbo[:, :], w["lbo"].partition_broadcast(P))
    for l in range(LAYERS):
        load(c1.qks[:, 0, l, :], w["qs"][l].partition_broadcast(P))
        load(c1.qks[:, 1, l, :], w["ks"][l].partition_broadcast(P))
        load(c1.wqkv[:, l, :], w["wqkv"][l])
        load(c1.wo[:, l, :, :], w["fwo"][l].rearrange("(a p) n -> p a n", p=P))
        load(c1.g1[:, l, :], w["g1"][l])
        load(c1.gb2[:, l, :], w["gb2"][l].partition_broadcast(P))
        load(c1.ln[:, 0, l:l + 1], w["lng"][l].unsqueeze(1))
        load(c1.ln[:, 1, l:l + 1], w["lnb"][l].unsqueeze(1))
        for i, (f0, rows) in enumerate(GCHUNKS):
            load(c1.g2[0:rows, l, i, :], w["g2"][l, f0:f0 + rows, :])
            load(c1.gb1[0:rows, l, 0, i:i + 1], w["gb1"][l, f0:f0 + rows].unsqueeze(1))
            load(c1.gb1[0:rows, l, 1, i:i + 1], w["gb1"][l, GLU + f0:GLU + f0 + rows].unsqueeze(1))
    return 16 * len(loads)


MM0 = 1 + 1 + 8 + 16 + 8 + 3
S0 = 4 * PAIRS0 + 27
PT0 = 4 * PAIRS0 + 27
O0 = PAIRS0 + EXPERTS
PASS0_CHAIN = LAYERNORM + 5 + PAIRS0 + 3


def pass0(nc, ctx, c, w, c1, x_all):
    def sb(name, shape):
        return ctx.enter_context(nc.sbuf_tensor(name, shape, FP32))

    def sem(name):
        return ctx.enter_context(nc.semaphore(name))

    wq, wk, wv = (sb(n, [P, HEADS0 * HD]) for n in ("wq", "wk", "wv"))
    wo = sb("wo", [P, PAIRS0, P])
    w1 = sb("w1", [P, EXPERTS + 1, FF])
    w3 = sb("w3", [P, EXPERTS + 1, FF])
    w2 = sb("w2", [P, EXPERTS + 1, 3, P])
    router = sb("router", [P, EXPERTS])
    bo = sb("bo", [P, P])
    xn = sb("xn", [P, TILES, P])
    xnT = sb("xnT", [P, TOK])
    v = sb("v", [P, TILES, HEADS0 * HD])
    q = sb("q", [P, 2, TOK])
    k = sb("k", [P, 2, TOK])
    attT = sb("attT", [P, PAIRS0, TOK])
    s_sb = sb("s_sb", [P, TOK])
    f_sb = sb("f_sb", [P, TOK])
    f_th = sb("f_th", [P, TOK])
    gate_in = sb("gate_in", [P, TILES, EXPERTS])
    best = sb("best", [P, TILES])
    best_th = sb("best_th", [P, TILES])
    hot = sb("hot", [P, TILES, EXPERTS])
    gates = sb("gates", [P, TILES, EXPERTS])
    gT = sb("gT", [EXPERTS, TOK])
    xg = sb("xg", [P, 2, TOK])
    th = sb("th", [P, 2, TOK])
    up = sb("up", [P, 2, TOK])
    mid = sb("mid", [P, 2, TOK])
    stats = sb("stats", [P, TILES, 6])
    mv = sb("mv", [P, TILES, 2])
    rstd = sb("rstd", [P, TILES])
    scratch = sb("scratch", [P, 2, 64])
    m = Buffers(q=q, k=k, v=v, p=sb("p", [P, RB, SB]), sm=sb("sm", [P, RB, SB]), pt=sb("pt", [P, 2, SB]),
              nmax=sb("nmax", [P, RB, 2]), den=sb("den", [P, 2, 4, 2]), rden=sb("rden", [P, 8]),
              o=sb("o", [P, 2, TILES, P]), mask=c.mask0, settled=c.settled, ident=c.ident,
              s_ps=c.ps[2:4], pt_ps=c.ps[4:6], o_ps=c.ps[6:8])
    mm_ps = c.ps[0:2]
    loaded = [sem(f"w_loaded{i}") for i in range(5)]
    mm_full, mm_done = sem("mm_full"), sem("mm_done")
    s_full, s_done = sem("s_full"), sem("s_done")
    pt_full, pt_done = sem("pt_full"), sem("pt_done")
    o_full, o_done = sem("o_full"), sem("o_done")
    xn_ready, gates_ready, best_ready, best_sig = (sem(n) for n in ("xn_ready", "gates_ready", "best_ready", "best_sig"))
    th_ready, mid_used = sem("th_ready"), sem("mid_used")
    s = Signals(exp_done=sem("exp_done"), pv_done=sem("pv_done"))
    chain, first_chain, x_done = sem("chain"), sem("first_chain"), sem("x_done")
    att = Attention(nc, PAIRS0, m, s)
    block = ctx.enter_context(nc.Block())

    def rings(it):
        r = {"mm": Ring(mm_full, mm_done, MM0, 2, it), "s": Ring(s_full, s_done, S0, 2, it),
             "pt": Ring(pt_full, pt_done, PT0, 2, it), "o": Ring(o_full, o_done, O0, 2, it),
             "exp": Ring(s.exp_done, None, 4 * PAIRS0, RB, it), "pt_of": {}, "o_of": {}}
        return r

    order = ["xnT", "scores"] + [("v", i) for i in range(8)] + attention_order(PAIRS0) + ["s", "gT", "f"]
    assert len(order) == MM0
    unit = {n: i for i, n in enumerate(order)}

    @block.sync
    def _(sp):
        for dst, src in ((wq, w["Wq"]), (wk, w["Wk"]), (wv, w["Wv"])):
            sp.dma_start(dst[:, :], src).then_inc(loaded[0], 16)
        sp.dma_start(router[:, :], w["router"]).then_inc(loaded[0], 16)
        sp.dma_start(wo[:, :, :], w["Wo"].rearrange("(a p) n -> p a n", p=P)).then_inc(loaded[1], 16)
        sp.dma_start(bo[:, :], w["bo0"].partition_broadcast(P)).then_inc(loaded[1], 16)
        for e in range(EXPERTS):
            sp.dma_start(w1[:, e, :], w["w1"][e]).then_inc(loaded[2], 16)
            sp.dma_start(w3[:, e, :], w["w3"][e]).then_inc(loaded[2], 16)
        sp.dma_start(w1[:, EXPERTS, :], w["ws1"]).then_inc(loaded[2], 16)
        sp.dma_start(w3[:, EXPERTS, :], w["ws3"]).then_inc(loaded[2], 16)
        for e in range(EXPERTS + 1):
            src = w["w2"][e] if e < EXPERTS else w["ws2"]
            sp.dma_start(w2[:, e, 0:2, :], src[0:2 * P, :].rearrange("(c p) n -> p c n", p=P)).then_inc(loaded[3], 16)
            sp.dma_start(w2[0:FF - 2 * P, e, 2, :], src[2 * P:FF, :]).then_inc(loaded[3], 16)
        c.PASS1_LOADS = load_pass1(sp, c1, w)

    @block.tensor
    def _(pe):
        pe.wait_ge(c.const_loaded, c.CONST_LOADS)
        pe.wait_ge(loaded[0], 4 * 16)
        pe.wait_ge(loaded[1], 2 * 16)
        with pe.Fori(0, LOOPS) as it:
            r = rings(it)
            mm = r["mm"]

            def mm_bank():
                kk = mm.take()
                pe.wait_ge(mm_done, mm.free(kk))
                return mm_ps[kk % 2]

            bank = mm_bank()
            pe.wait_ge(xn_ready, it + 1)
            for t in range(TILES):
                last = nc.tensor.transpose(bank[:, t * P:(t + 1) * P], xn[:, t, :], c.ident[:, :])
            last.then_inc(mm_full, 1)
            bank = mm_bank()
            pe.wait_ge(mm_done, mm.done(unit["xnT"]))
            for t in range(TILES):
                last = nc.tensor.matmul(bank[:, t * EXPERTS:(t + 1) * EXPERTS], xnT[:, t * P:(t + 1) * P],
                                        router[:, :], start=True, stop=True)
            last.then_inc(mm_full, 1)
            for t in range(TILES):
                for half in range(2):
                    bank = mm_bank()
                    nc.tensor.matmul(bank[:, :], xnT[:, t * P:(t + 1) * P], wv[:, half * 512:(half + 1) * 512],
                                     start=True, stop=True).then_inc(mm_full, 1)

            def produce(which, pair):
                bank_ = mm_bank()
                nc.tensor.matmul(bank_[:, :], (wq, wk)[which][:, pair * P:(pair + 1) * P], xnT[:, :],
                                 start=True, stop=True).then_inc(mm_full, 1)

            def merge(pair):
                bank_ = mm_bank()
                for t in range(TILES):
                    last_ = nc.tensor.transpose(bank_[:, t * P:(t + 1) * P], m.o[:, pair % 2, t, :], c.ident[:, :])
                last_.then_inc(mm_full, 1)

            r["qk_done"] = [mm.done(unit[("k", p)]) for p in range(PAIRS0)]
            att.tensor(pe, it, r, produce, merge, 0)
            bank = mm_bank()
            pe.wait_ge(mm_done, mm.done(unit[("merge", PAIRS0 - 1)]))
            for t in range(TILES):
                for pair in range(PAIRS0):
                    last = nc.tensor.matmul(bank[:, t * P:(t + 1) * P], attT[:, pair, t * P:(t + 1) * P],
                                            wo[:, pair, :], start=pair == 0, stop=pair == PAIRS0 - 1)
            last.then_inc(mm_full, 1)
            bank = mm_bank()
            pe.wait_ge(gates_ready, it + 1)
            for t in range(TILES):
                last = nc.tensor.transpose(bank[0:EXPERTS, t * P:(t + 1) * P], gates[:, t, :], c.ident[:, :])
            last.then_inc(mm_full, 1)
            f_bank = mm_bank()
            pe.wait_ge(mm_done, mm.done(unit["gT"]))
            pe.wait_ge(loaded[2], 18 * 16)
            pe.wait_ge(loaded[3], 18 * 16)
            n = 0
            mid_ok, row_ok = [], []

            def gate_row(e):
                kk = r["o"].take()
                pe.wait_ge(o_done, r["o"].free(kk))
                row_ok.append(r["o"].done(kk))
                nc.tensor.matmul(m.o_ps[kk % 2][:, :], c.sel[0:EXPERTS, e, :], gT[:, :],
                                 start=True, stop=True).then_inc(o_full, 1)

            def down(i):
                e_, ch = i // 3, i % 3
                rows = FCHUNKS[ch][1]
                pe.wait_ge(pt_done, mid_ok[i])
                for t in range(TILES):
                    last_ = nc.tensor.matmul(f_bank[:, t * P:(t + 1) * P], mid[0:rows, i % 2, t * P:(t + 1) * P],
                                             w2[0:rows, e_, ch, :], start=i == 0 and t == 0, stop=i == 26,
                                             skip_group_check=True)
                return last_

            gate_row(0)
            for e in range(EXPERTS + 1):
                if e + 1 < EXPERTS:
                    gate_row(e + 1)
                if e < EXPERTS:
                    pe.wait_ge(o_done, row_ok[e])
                src = xg[:, e % 2, :] if e < EXPERTS else xnT[:, :]
                for f0, rows in FCHUNKS:
                    ks, kp = r["s"].take(), r["pt"].take()
                    pe.wait_ge(s_done, r["s"].free(ks))
                    nc.tensor.matmul(m.s_ps[ks % 2][0:rows, :], w1[:, e, f0:f0 + rows], src,
                                     start=True, stop=True).then_inc(s_full, 1)
                    pe.wait_ge(pt_done, r["pt"].free(kp))
                    mid_ok.append(r["pt"].done(kp))
                    nc.tensor.matmul(m.pt_ps[kp % 2][0:rows, :], w3[:, e, f0:f0 + rows], src,
                                     start=True, stop=True).then_inc(pt_full, 1)
                    n += 1
                    if n >= 2:
                        down(n - 2).then_inc(mid_used, 1)
            down(26).then_inc(mm_full, 1)
            for x in ("mm", "s", "pt", "o"):
                r[x].close()

    @block.scalar
    def _(act):
        act.sem_inc(mm_done, 1)
        with act.Fori(0, LOOPS) as it:
            r = rings(it)
            mm = r["mm"]

            def mm_bank():
                kk = mm.take()
                act.wait_ge(mm_full, mm.full(kk))
                return mm_ps[kk % 2]

            bank = mm_bank()
            nc.scalar.activation(xnT[:, :], bank[:, :], ACT.Copy).then_inc(mm_done, 1)
            bank = mm_bank()
            nc.scalar.activation(gate_in[:, :, :].rearrange("p t e -> p (t e)"), bank[:, 0:TILES * EXPERTS],
                                 ACT.Copy).then_inc(mm_done, 1)
            act.wait_ge(best_ready, it + 1)
            nc.scalar.activation(best_th[:, :], best[:, :], ACT.Tanh, scale=0.5).then_inc(best_sig, 1)
            for t in range(TILES):
                for half in range(2):
                    bank = mm_bank()
                    nc.scalar.activation(v[:, t, half * 512:(half + 1) * 512], bank[:, :], ACT.Copy)\
                        .then_inc(mm_done, 1)

            def produce(which, pair):
                bank_ = mm_bank()
                nc.scalar.activation((q, k)[which][:, pair % 2, :], bank_[:, :], ACT.Copy).then_inc(mm_done, 1)

            def merge(pair):
                bank_ = mm_bank()
                nc.scalar.activation(attT[:, pair, :], bank_[:, :], ACT.Copy).then_inc(mm_done, 1)

            att.scalar(act, it, r, produce, merge, 0)
            bank = mm_bank()
            nc.scalar.activation(s_sb[:, :], bank[:, :], ACT.Copy).then_inc(mm_done, 1)
            bank = mm_bank()
            nc.scalar.activation(gT[:, :], bank[0:EXPERTS, :], ACT.Copy).then_inc(mm_done, 1)
            for i in range(27):
                rows = FCHUNKS[i % 3][1]
                ks = r["s"].take()
                act.wait_ge(s_full, r["s"].full(ks))
                if i >= 2:
                    act.wait_ge(s_done, r["s"].done(ks - 2))
                nc.scalar.activation(th[0:rows, i % 2, :], m.s_ps[ks % 2][0:rows, :], ACT.Tanh, scale=0.5)\
                    .then_inc(th_ready, 1)
            bank = mm_bank()
            nc.scalar.activation(f_th[:, :], bank[:, :], ACT.Tanh, scale=0.25)
            nc.scalar.activation(f_sb[:, :], bank[:, :], ACT.Copy).then_inc(mm_done, 1)
            mm.close()

    @block.vector
    def _(dve):
        for done in (s_done, pt_done, o_done):
            dve.sem_inc(done, 1)
        dve.wait_ge(c.x_loaded, 16 * c.X_LOADS)
        dve.wait_ge(c.const_loaded, c.CONST_LOADS)
        dve.wait_ge(loaded[1], 2 * 16)
        layernorm(nc, c, Chain(dve, first_chain, LAYERNORM, 0), lambda t: xn[:, t, :], lambda t: x_all[:, t, :],
                  stats, mv, rstd, scratch).then_inc(xn_ready, 1)
        with dve.Fori(0, LOOPS) as it:
            r = rings(it)
            mm = r["mm"]
            link = Chain(dve, chain, PASS0_CHAIN, it)
            r["link"] = link
            r["merged"] = lambda pair: mm.full(unit[("merge", pair)])
            xt = lambda t: x_all[:, bass.ds(it * TILES + t, 1), :].rearrange("p o d -> p (o d)")
            dve.wait_ge(mm_done, mm.done(unit["scores"]))
            nc.vector.tensor_reduce(best[:, :], gate_in[:, :, :], axis=AX.X, op=ALU.max).then_inc(best_ready, 1)
            dve.wait_ge(best_ready, it + 1)
            wide = lambda a: a.unsqueeze(2).to_broadcast([P, TILES, EXPERTS])
            link(nc.vector.tensor_tensor(hot[:, :, :], gate_in[:, :, :], wide(best[:, :]), ALU.is_equal))
            link(nc.vector.tensor_tensor(hot[:, :, :], hot[:, :, :], c.rank[:, :].unsqueeze(1).to_broadcast([P, TILES, EXPERTS]), ALU.mult))
            link(nc.vector.tensor_reduce(scratch[:, 0, 0:TILES], hot[:, :, :], axis=AX.X, op=ALU.max))
            link(nc.vector.tensor_tensor(hot[:, :, :], hot[:, :, :], wide(scratch[:, 0, 0:TILES]), ALU.is_equal))
            dve.wait_ge(best_sig, it + 1)
            link(nc.vector.tensor_scalar(scratch[:, 1, 0:TILES], best_th[:, :], 0.5, 0.5, ALU.mult, ALU.add))
            nc.vector.tensor_tensor(gates[:, :, :], hot[:, :, :], wide(scratch[:, 1, 0:TILES]), ALU.mult)\
                .then_inc(gates_ready, 1)
            att.vector(dve, it, r, lambda seq, pair, h, i: -0.125, 0)
            def gated(e):
                kk = r["o"].take()
                dve.wait_ge(o_full, it * EXPERTS + (e + 1))
                if e >= 2:
                    dve.wait_ge(pt_full, r["pt"].full(4 * PAIRS0 + 3 * (e - 2) + 2))
                nc.vector.tensor_tensor(xg[:, e % 2, :], xnT[:, :], m.o_ps[kk % 2][:, :], ALU.mult)\
                    .then_inc(o_done, 1)

            dve.wait_ge(mm_done, mm.done(unit["xnT"]))
            gated(0)
            for e in range(EXPERTS + 1):
                if e + 1 < EXPERTS:
                    gated(e + 1)
                if e == 2:
                    layernorm(nc, c, link, lambda t: xn[:, t, :], lambda t: xt(TILES + t), stats, mv, rstd, scratch)\
                        .then_inc(xn_ready, 1)
                for ch in range(3):
                    i = 3 * e + ch
                    rows = FCHUNKS[ch][1]
                    ks, kp = r["s"].take(), r["pt"].take()
                    dve.wait_ge(th_ready, it * 27 + (i + 1))
                    nc.vector.scalar_tensor_tensor(out=up[0:rows, i % 2, :], in0=th[0:rows, i % 2, :], scalar=1.0,
                                                   in1=m.s_ps[ks % 2][0:rows, :], op0=ALU.add, op1=ALU.mult)\
                        .then_inc(s_done, 1)
                    dve.wait_ge(s_done, r["s"].done(ks))
                    dve.wait_ge(pt_full, r["pt"].full(kp))
                    if i >= 2:
                        dve.wait_ge(mid_used, it * 26 + (i - 1))
                    nc.vector.tensor_tensor(mid[0:rows, i % 2, :], up[0:rows, i % 2, :], m.pt_ps[kp % 2][0:rows, :], ALU.mult)\
                        .then_inc(pt_done, 1)
            dve.wait_ge(mm_done, mm.done(unit["f"]))
            four = lambda a: a.rearrange("p (t d) -> p t d", t=TILES)
            link(nc.vector.tensor_tensor(four(s_sb[:, :]), four(s_sb[:, :]), bo[:, :].unsqueeze(1).to_broadcast([P, TILES, P]), ALU.add))
            link(nc.vector.scalar_tensor_tensor(out=f_th[:, :], in0=f_th[:, :], scalar=1.0, in1=f_sb[:, :],
                                                op0=ALU.add, op1=ALU.mult))
            link(nc.vector.tensor_tensor(f_th[:, :], f_th[:, :], s_sb[:, :], ALU.mult))
            for t in range(TILES):
                last = nc.vector.scalar_tensor_tensor(out=xt(t), in0=f_th[:, t * P:(t + 1) * P], scalar=0.25,
                                                      in1=xt(t), op0=ALU.mult, op1=ALU.add)
            last.then_inc(x_done, 1)
            link.close()


MM1 = 1 + 2 + LAYERS * (12 + 3 * PAIRS1 + 4 + 3) + LAYERS - 1
S1 = TILES + 3 * TILES + LAYERS * (4 * PAIRS1 + 3)
PT1 = LAYERS * 4 * PAIRS1
O1 = LAYERS * PAIRS1
PASS1_CHAIN = LAYERNORM + 3 * TILES + 2 + LAYERS * (TILES + 1 + NEWTON + PAIRS1 + LAYERNORM + 1) + 3


KN_VECTOR = 2
CUM_FROM = 2


def pass1(nc, ctx, c, c1, x_all, x_out):
    def sb(name, shape):
        return ctx.enter_context(nc.sbuf_tensor(name, shape, FP32))

    def sem(name):
        return ctx.enter_context(nc.semaphore(name))

    lw, lwo, lb, lbo, wqkv, wo = c1.lw, c1.lwo, c1.lb, c1.lbo, c1.wqkv, c1.wo
    g1, g2, gb1, gb2, ln = c1.g1, c1.g2, c1.gb1, c1.gb2, c1.ln
    tri, rot, qks = c1.tri, c1.rot, c1.qks
    rots = sb("rots", [P, LAYERS, 2, 2, 2, HD])
    xn = sb("xn1", [P, TILES, P])
    xT = sb("xT", [P, TOK])
    hT = sb("hT", [P, TOK])
    qkb = sb("qkb", [P, TILES, 2 * P])
    mn = sb("mn", [P, TILES, 2 * P])
    phi = qkb
    v9 = sb("v9", [P, TILES, LH, LE])
    shared = sb("shared", [P, (PAIRS1 + 6) * TOK])
    kv = shared[:, 0:TILES * LH * LD * LE].rearrange("p (t n) -> p t n", t=TILES)
    pr = sb("pr", [P, 6 * LD * LE])
    nd = sb("nd", [P, TILES, LH * LE])
    o1 = sb("o1", [P, TILES, P])
    oT = xT
    s1 = sb("s1", [P, TOK])
    raw = sb("raw", [P, TILES, 2 * INNER1])
    sq = sb("sq", [P, TILES, 2 * INNER1])
    qkr = sb("qkr", [P, TILES, 2 * INNER1])
    ss = sb("ss", [P, TILES * 2 * HEADS1])
    rr = sb("rr", [P, TILES * 2 * HEADS1])
    nrq = sb("nrq", [P, TILES, HEADS1])
    v = sb("v1", [P, TILES, INNER1])
    q = sb("q1", [P, 2, TOK])
    k = sb("k1", [P, 2, TOK])
    attT = shared[:, 0:PAIRS1 * TOK].rearrange("p (a n) -> p a n", a=PAIRS1)
    y = sb("y", [P, TILES, P])
    xa = sb("xa", [P, TILES, P])
    xb = sb("xb", [P, TILES, P])
    h = sb("h", [P, TILES, P])
    yT = sb("yT", [P, TOK])
    gl, glu = (shared[:, (PAIRS1 + a) * TOK:(PAIRS1 + a + 3) * TOK].rearrange("p (a n) -> p a n", a=3) for a in (0, 3))
    f_th = y
    stats = sb("stats1", [P, TILES, 6])
    mv = sb("mv1", [P, TILES, 2])
    rstd = sb("rstd1", [P, TILES])
    scratch = sb("scratch1", [P, 2, 64])
    m = Buffers(q=q, k=k, v=v, p=sb("p1", [P, RB, SB]), sm=sb("sm1", [P, RB, SB]), pt=sb("pt1", [P, 2, SB]),
              nmax=sb("nmax1", [P, RB, 2]), den=sb("den1", [P, 2, 4, 2]), rden=sb("rden1", [P, 8]),
              o=sb("o_1", [P, 2, TILES, P]), mask=c.mask1, settled=c.settled, ident=c.ident,
              s_ps=c.ps[2:4], pt_ps=c.ps[4:6], o_ps=c.ps[6:8])
    mm_ps = c.ps[0:2]
    loaded, LOADED = c1.loaded, c.PASS1_LOADS
    mm_full, mm_done = sem("mm1_full"), sem("mm1_done")
    s_full, s_done = sem("s1_full"), sem("s1_done")
    pt_full, pt_done = sem("pt1_full"), sem("pt1_done")
    o_full, o_done = sem("o1_full"), sem("o1_done")
    s = Signals(exp_done=sem("exp1_done"), pv_done=sem("pv1_done"))
    chain, first_chain = sem("chain1"), sem("first_chain1")
    tables_ready, ones_ready, zero_ready = sem("tables_ready"), sem("ones_ready"), sem("zero_ready")
    xn_ready, mn_ready, ex_ready, phi_ready, kv_ready = (sem(n + "_ready") for n in ("xn1", "mn", "ex", "phi", "kv"))
    o1_ready, t2_ready, rot_ready, r_ready, kn_ready = (sem(n + "_ready") for n in ("o1", "t2", "rot", "r", "kn"))
    x2_ready, hn_ready, x3_ready, th_ready, out_ready = (sem(n + "_ready") for n in ("x2", "hn", "x3", "th1", "out"))
    att = Attention(nc, PAIRS1, m, s)

    order = ["xT"]
    for l in range(LAYERS):
        order += [("raw", l, t, i) for t in range(TILES) for i in range(3)]
        order += [(n, l, p) for n, p in attention_order(PAIRS1)]
        order += [("wo", l)] + (["oT", "s1"] if l == 0 else [])
        order += [("shift", l), ("yT", l)] + [("g", l, i) for i in range(3)] + [("down", l)]
        order += [("hT", l + 1)] if l + 1 < LAYERS else []
    assert len(order) == MM1, (len(order), MM1)
    unit = {n: i for i, n in enumerate(order)}
    S_LIN = 0
    S_ATT = [TILES, TILES + 3 * TILES + 4 * PAIRS1 + 3]
    LAYER_UNITS = 4 * PAIRS1

    def rings(it):
        return {"mm": Ring(mm_full, mm_done, MM1, 2, it), "s": Ring(s_full, s_done, S1, 2, it),
                "pt": Ring(pt_full, pt_done, PT1, 2, it), "o": Ring(o_full, o_done, O1, 2, it),
                "exp": Ring(s.exp_done, None, LAYERS * LAYER_UNITS, RB, it), "pt_of": {}, "o_of": {}}

    def k_over_norm(eng, t):
        kk = qkr[:, t, INNER1:2 * INNER1].rearrange("p (h d) -> p h d", h=HEADS1)
        at = (t * 2 + 1) * HEADS1
        return eng.tensor_tensor(kk, kk, rr[:, at:at + HEADS1].unsqueeze(2).to_broadcast([P, HEADS1, HD]), ALU.mult)

    block = ctx.enter_context(nc.Block())

    @block.sync
    def _(sp):
        out = x_out.rearrange("n (t p) d -> p (n t) d", p=P)
        with sp.Fori(0, LOOPS) as it:
            sp.wait_ge(out_ready, it + 1)
            sp.dma_start(out[:, bass.ds(it * TILES, TILES), :], x_all[:, bass.ds(it * TILES, TILES), :])\
                .then_inc(c.stored, 16)
        sp.wait_ge(c.stored, 16 * LOOPS)

    @block.tensor
    def _(pe):
        pe.wait_ge(loaded, LOADED)
        with pe.Fori(0, LOOPS) as it:
            r = rings(it)
            mm = r["mm"]

            def mm_bank():
                kk = mm.take()
                pe.wait_ge(mm_done, mm.free(kk))
                return mm_ps[kk % 2]

            def to_features(src):
                bank_ = mm_bank()
                for t_ in range(TILES):
                    last_ = nc.tensor.transpose(bank_[:, t_ * P:(t_ + 1) * P], src[:, t_, :], c.ident[:, :])
                last_.then_inc(mm_full, 1)

            pe.wait_ge(xn_ready, it + 1)
            to_features(xn)
            pe.wait_ge(mm_done, mm.done(unit["xT"]))
            for t in range(TILES):
                kk = r["s"].take()
                pe.wait_ge(s_done, r["s"].free(kk))
                nc.tensor.matmul(m.s_ps[kk % 2][:, 0:3 * P], xT[:, t * P:(t + 1) * P],
                                 lw[:, :, :].rearrange("p a n -> p (a n)"), start=True, stop=True).then_inc(s_full, 1)
            for l in range(LAYERS):
                if l:
                    pe.wait_ge(mm_done, mm.done(unit[("hT", l)]))
                for t in range(TILES):
                    for i in range(3):
                        bank = mm_bank()
                        nc.tensor.matmul(bank[:, :], hT[:, t * P:(t + 1) * P],
                                         wqkv[:, l, i * INNER1:(i + 1) * INNER1], start=True, stop=True)\
                            .then_inc(mm_full, 1)
                def running_sums(u):
                    if not CUM_FROM <= u < CUM_FROM + 3 * TILES:
                        return
                    t, part = (u - CUM_FROM) // 3, (u - CUM_FROM) % 3
                    if part == 0:
                        pe.wait_ge(kv_ready, it * TILES + (t + 1))
                    h0, nh = LCHUNKS[part]
                    kk = r["s"].take()
                    pe.wait_ge(s_done, r["s"].free(kk))
                    a, n = h0 * LD * LE, nh * LD * LE
                    last_ = nc.tensor.matmul(m.s_ps[kk % 2][:, 0:n], tri[:, 0, :], kv[:, t, a:a + n],
                                             start=True, stop=t % 2 == 0)
                    if t % 2:
                        last_ = nc.tensor.matmul(m.s_ps[kk % 2][:, 0:n], tri[:, 1, :], kv[:, t - 1, a:a + n],
                                                 start=False, stop=True)
                    last_.then_inc(s_full, 1)

                def produce(which, pair):
                    if pair == 0:
                        if which == 0:
                            pe.wait_ge(rot_ready, it * 2 * LAYERS * TILES + 2 * (l + 1) * TILES)
                        else:
                            pe.wait_ge(kn_ready, it * LAYERS * TILES + (l + 1) * TILES)
                    bank_ = mm_bank()
                    a = which * INNER1 + pair * P
                    for t_ in range(TILES):
                        last_ = nc.tensor.transpose(bank_[:, t_ * P:(t_ + 1) * P], qkr[:, t_, a:a + P], c.ident[:, :])
                    last_.then_inc(mm_full, 1)

                def merge(pair):
                    to_features(m.o[:, pair % 2, :, :])

                r["qk_done"] = [mm.done(unit[("k", l, p)]) for p in range(PAIRS1)]
                att.tensor(pe, it, r, produce, merge, l * LAYER_UNITS, running_sums if l == 0 else None)
                bank = mm_bank()
                pe.wait_ge(mm_done, mm.done(unit[("merge", l, PAIRS1 - 1)]))
                for t in range(TILES):
                    for pair in range(PAIRS1):
                        last = nc.tensor.matmul(bank[:, t * P:(t + 1) * P], attT[:, pair, t * P:(t + 1) * P],
                                                wo[:, l, pair, :], start=pair == 0, stop=pair == PAIRS1 - 1)
                last.then_inc(mm_full, 1)
                if l == 0:
                    pe.wait_ge(o1_ready, it + 1)
                    to_features(o1)
                    bank = mm_bank()
                    pe.wait_ge(mm_done, mm.done(unit["oT"]))
                    for t in range(TILES):
                        last = nc.tensor.matmul(bank[:, t * P:(t + 1) * P], oT[:, t * P:(t + 1) * P], lwo[:, :],
                                                start=True, stop=True)
                    last.then_inc(mm_full, 1)
                bank = mm_bank()
                pe.wait_ge(x2_ready, it * LAYERS + (l + 1))
                for t in range(TILES):
                    o = bank[:, t * HD:(t + 1) * HD]
                    last = nc.tensor.matmul(o, tri[:, 2, :], xa[:, t, HD:P], start=True, stop=t % 2 == 0)
                    if t % 2:
                        last = nc.tensor.matmul(o, tri[:, 3, :], xa[:, t - 1, HD:P], start=False, stop=True)
                last.then_inc(mm_full, 1)
                pe.wait_ge(hn_ready, it * LAYERS + (l + 1))
                to_features(h)
                pe.wait_ge(mm_done, mm.done(unit[("yT", l)]))
                for i, (f0, rows) in enumerate(GCHUNKS):
                    bank = mm_bank()
                    nc.tensor.matmul(bank[0:rows, :], g1[:, l, GLU + f0:GLU + f0 + rows], yT[:, :],
                                     start=True, stop=True).then_inc(mm_full, 1)
                    kk = r["s"].take()
                    pe.wait_ge(s_done, r["s"].free(kk))
                    nc.tensor.matmul(m.s_ps[kk % 2][0:rows, :], g1[:, l, f0:f0 + rows], yT[:, :],
                                     start=True, stop=True).then_inc(s_full, 1)
                bank = mm_bank()
                pe.wait_ge(s_done, r["s"].done(kk))
                for t in range(TILES):
                    for i, (f0, rows) in enumerate(GCHUNKS):
                        last = nc.tensor.matmul(bank[:, t * P:(t + 1) * P], glu[0:rows, i, t * P:(t + 1) * P],
                                                g2[0:rows, l, i, :], start=i == 0, stop=i == 2)
                last.then_inc(mm_full, 1)
                if l + 1 < LAYERS:
                    pe.wait_ge(x3_ready, it * LAYERS + (l + 1))
                    to_features(xb)
            for x in ("mm", "s", "pt", "o"):
                r[x].close()

    @block.scalar
    def _(act):
        act.sem_inc(mm_done, 1)
        act.wait_ge(loaded, LOADED)
        act.wait_ge(zero_ready, 1)
        with act.Fori(0, LOOPS) as it:
            r = rings(it)
            mm = r["mm"]

            def mm_bank():
                kk = mm.take()
                act.wait_ge(mm_full, mm.full(kk))
                return mm_ps[kk % 2]

            def evacuate(dst):
                nc.scalar.activation(dst, mm_bank()[:, :], ACT.Copy).then_inc(mm_done, 1)

            def shifted(bank_):
                nc.scalar.activation(hT[0:HD, :], bank_[0:HD, :], ACT.Copy)
                two = lambda a: a.rearrange("p (s t) -> p s t", s=2)
                nc.scalar.activation(two(hT[HD:P, :])[:, :, 1:SEQ], two(bank_[HD:P, :])[:, :, 0:SEQ - 1], ACT.Copy)\
                    .then_inc(mm_done, 1)

            bank = mm_bank()
            nc.scalar.activation(xT[:, :], bank[:, :], ACT.Copy)
            shifted(bank)
            for l in range(LAYERS):
                for t in range(TILES):
                    for i in range(2):
                        bank = mm_bank()
                        a = i * INNER1
                        nc.scalar.activation(sq[:, t, a:a + INNER1], bank[:, :], ACT.Square)
                        nc.scalar.activation(raw[:, t, a:a + INNER1], bank[:, :], ACT.Copy).then_inc(mm_done, 1)
                    evacuate(v[:, t, :])
                    if l == 0:
                        act.wait_ge(mn_ready, it * TILES + (t + 1))
                        nc.scalar.activation(mn[:, t, :], mn[:, t, :], ACT.Exp).then_inc(ex_ready, 1)
                r["s"].k, r["pt"].k = S_ATT[l], l * LAYER_UNITS
                att.scalar(act, it, r, lambda which, pair: evacuate((q, k)[which][:, pair % 2, :]),
                           lambda pair: evacuate(attT[:, pair, :]), l * LAYER_UNITS,
                           lambda u: r["s"].take() if l == 0 and CUM_FROM <= u < CUM_FROM + 3 * TILES else None)
                evacuate(y[:, :, :].rearrange("p t d -> p (t d)"))
                if l == 0:
                    evacuate(oT[:, :])
                    evacuate(s1[:, :])
                bank = mm_bank()
                nc.scalar.activation(h[:, :, HD:P], bank[:, 0:TILES * HD].rearrange("p (t d) -> p t d", t=TILES),
                                     ACT.Copy).then_inc(mm_done, 1)
                bank = mm_bank()
                nc.scalar.activation(yT[:, :], bank[:, :], ACT.Identity, scale=ln[:, 0, l:l + 1],
                                     bias=ln[:, 1, l:l + 1]).then_inc(mm_done, 1)
                for i, (f0, rows) in enumerate(GCHUNKS):
                    bank = mm_bank()
                    nc.scalar.activation(gl[0:rows, i, :], bank[0:rows, :], ACT.Gelu, bias=gb1[0:rows, l, 1, i:i + 1])\
                        .then_inc(mm_done, 1)
                evacuate(y[:, :, :].rearrange("p t d -> p (t d)"))
                if l + 1 < LAYERS:
                    shifted(mm_bank())
            act.wait_ge(x3_ready, it * LAYERS + LAYERS)
            nc.scalar.activation(f_th[:, :, :], xb[:, :, :], ACT.Tanh, scale=0.5).then_inc(th_ready, 1)
            mm.close()

    @block.gpsimd
    def _(pool):
        pool.memset(v9[:, :, :, LD:LE], 1.0).then_inc(ones_ready, 1)
        pool.memset(hT[:, 0:1], 0.0)
        pool.memset(hT[:, SEQ:SEQ + 1], 0.0).then_inc(zero_ready, 1)
        pool.wait_ge(tables_ready, 1)
        with pool.Fori(0, LOOPS) as it:
            s_at = Ring(s_full, s_done, S1, 2, it)
            mm = Ring(mm_full, mm_done, MM1, 2, it)
            for t in range(TILES):
                pool.wait_ge(s_done, s_at.done(S_LIN + t))
                pool.sem_inc(c.settled_pool, 1)
                nc.gpsimd.tensor_scalar(mn[:, t, :], qkb[:, t, :], 0.0, None, ALU.min).then_inc(mn_ready, 1)
            for l in range(LAYERS):
                for t in range(TILES):
                    pool.wait_ge(mm_done, mm.done(unit[("raw", l, t, 1)]))
                    pool.wait_ge(rot_ready, it * 2 * LAYERS * TILES + (2 * l * TILES + 2 * t + 1))
                    src = raw[:, t, :].rearrange("p (a h d) -> p a h d", a=2, h=HEADS1)
                    dst = sq[:, t, :].rearrange("p (a h d) -> p a h d", a=2, h=HEADS1)
                    tab = rots[:, l, t % 2, 1, :, :].unsqueeze(2).to_broadcast([P, 2, HEADS1, HD])
                    H2 = HD // 2
                    nc.gpsimd.tensor_tensor(dst[:, :, :, 0:H2], src[:, :, :, H2:HD], tab[:, :, :, 0:H2], ALU.mult)
                    nc.gpsimd.tensor_tensor(dst[:, :, :, H2:HD], src[:, :, :, 0:H2], tab[:, :, :, H2:HD], ALU.mult)\
                        .then_inc(t2_ready, 1)
                for t in range(KN_VECTOR, TILES):
                    pool.wait_ge(r_ready, it * LAYERS + (l + 1))
                    k_over_norm(nc.gpsimd, t).then_inc(kn_ready, 1)
                if l == 0:
                    for t in range(TILES):
                        pool.wait_ge(phi_ready, it * TILES + (t + 1))
                        kk = phi[:, t, P:2 * P].rearrange("p (h d) -> p h d", h=LH).unsqueeze(3)\
                            .to_broadcast([P, LH, LD, LE])
                        vv = v9[:, t, :, :].unsqueeze(2).to_broadcast([P, LH, LD, LE])
                        nc.gpsimd.tensor_tensor(kv[:, t, :].rearrange("p (h d e) -> p h d e", h=LH, d=LD), kk, vv,
                                                ALU.mult).then_inc(kv_ready, 1)

    @block.vector
    def _(dve):
        for done in (s_done, pt_done, o_done):
            dve.sem_inc(done, 1)
        dve.wait_ge(loaded, LOADED)
        dve.wait_ge(ones_ready, 1)
        H2 = HD // 2
        for l in range(LAYERS):
            for a in range(2):
                sc = lambda lo, hi: qks[:, a, l, lo:hi].unsqueeze(1).to_broadcast([P, 2, hi - lo])
                nc.vector.tensor_tensor(rots[:, l, :, 0, a, :], rot[:, :, 0, a, :], sc(0, HD), ALU.mult)
                nc.vector.tensor_tensor(rots[:, l, :, 1, a, 0:H2], rot[:, :, 1, a, 0:H2], sc(H2, HD), ALU.mult)
                last = nc.vector.tensor_tensor(rots[:, l, :, 1, a, H2:HD], rot[:, :, 1, a, H2:HD], sc(0, H2), ALU.mult)
        last.then_inc(tables_ready, 1)
        dve.wait_ge(tables_ready, 1)
        layernorm(nc, c, Chain(dve, first_chain, LAYERNORM, 0), lambda t: xn[:, t, :], lambda t: x_all[:, t, :],
                  stats, mv, rstd, scratch).then_inc(xn_ready, 1)
        with dve.Fori(0, LOOPS) as it:
            r = rings(it)
            mm = r["mm"]
            link = Chain(dve, chain, PASS1_CHAIN, it)
            r["link"] = link
            xt = lambda t: x_all[:, bass.ds(it * TILES + t, 1), :].rearrange("p o d -> p (o d)")
            for t in range(TILES):
                kk = r["s"].take()
                dve.wait_ge(s_full, r["s"].full(kk))
                bank = m.s_ps[kk % 2]
                nc.vector.tensor_tensor(qkb[:, t, :], bank[:, 0:2 * P], lb[:, 0:2, :].rearrange("p a n -> p (a n)"), ALU.add)
                nc.vector.tensor_tensor(v9[:, t, :, 0:LD], bank[:, 2 * P:3 * P].rearrange("p (h d) -> p h d", h=LH),
                                        lb[:, 2, :].rearrange("p (h d) -> p h d", h=LH), ALU.add).then_inc(s_done, 1)
            for l in range(LAYERS):
                for t in range(TILES):
                    dve.wait_ge(mm_done, mm.done(unit[("raw", l, t, 1)]))
                    at = t * 2 * HEADS1
                    nc.vector.tensor_reduce(ss[:, at:at + 2 * HEADS1], sq[:, t, :].rearrange("p (g d) -> p g d", d=HD),
                                            axis=AX.X, op=ALU.add).then_inc(rot_ready, 1)
                    four = lambda a: a.rearrange("p (a h d) -> p a h d", a=2, h=HEADS1)
                    link(nc.vector.tensor_tensor(four(qkr[:, t, :]), four(raw[:, t, :]),
                                                 rots[:, l, t % 2, 0, :, :].unsqueeze(2).to_broadcast([P, 2, HEADS1, HD]),
                                                 ALU.mult))
                    if l == 0:
                        dve.wait_ge(ex_ready, it * TILES + (t + 1))
                        nc.vector.scalar_tensor_tensor(out=phi[:, t, :], in0=qkb[:, t, :], scalar=0.0, in1=mn[:, t, :],
                                                       op0=ALU.max, op1=ALU.add).then_inc(phi_ready, 1)
                    dve.wait_ge(t2_ready, it * LAYERS * TILES + (l * TILES + t + 1))
                    nc.vector.tensor_tensor(qkr[:, t, :], qkr[:, t, :], sq[:, t, :], ALU.add).then_inc(rot_ready, 1)
                link(nc.vector.tensor_scalar(ss[:, :], ss[:, :], 1e-24, None, ALU.max))
                newton_rsqrt(nc, link, rr[:, :], ss[:, :], scratch[:, 0, :])
                nc.vector.tensor_scalar(nrq[:, :, :], rr[:, :].rearrange("p (t a h) -> p t a h", t=TILES, a=2)[:, :, 0, :],
                                        -8.0, None, ALU.mult).then_inc(r_ready, 1)
                dve.wait_ge(r_ready, it * LAYERS + (l + 1))
                for t in range(KN_VECTOR):
                    k_over_norm(nc.vector, t).then_inc(kn_ready, 1)

                def linear_terms(u):
                    if CUM_FROM <= u < CUM_FROM + 3 * TILES:
                        t, part = (u - CUM_FROM) // 3, (u - CUM_FROM) % 3
                        h0, nh = LCHUNKS[part]
                        kk = r["s"].take()
                        dve.wait_ge(s_full, r["s"].full(kk))
                        n = nh * LD * LE
                        src = m.s_ps[kk % 2][:, 0:n].rearrange("p (h d e) -> p h e d", h=nh, d=LD)
                        dst = pr[:, 0:n].rearrange("p (h e d) -> p h e d", h=nh, e=LE)
                        qq = phi[:, t, h0 * LD:(h0 + nh) * LD].rearrange("p (h d) -> p h d", h=nh)\
                            .unsqueeze(2).to_broadcast([P, nh, LE, LD])
                        nc.vector.tensor_tensor(dst, src, qq, ALU.mult).then_inc(s_done, 1)
                        dve.wait_ge(s_done, r["s"].done(kk))
                        link(nc.vector.tensor_reduce(nd[:, t, h0 * LE:(h0 + nh) * LE],
                                                     pr[:, 0:n].rearrange("p (g d) -> p g d", d=LD),
                                                     axis=AX.X, op=ALU.add))
                    if u == CUM_FROM + 3 * TILES - 1:
                        nd4 = nd[:, :, :].rearrange("p t (h e) -> p t h e", h=LH)
                        den = scratch[:, 0, :].rearrange("p (t h) -> p t h", t=TILES)
                        link(nc.vector.tensor_scalar(den, nd4[:, :, :, LD], 1e-6, None, ALU.add))
                        link(nc.vector.reciprocal(scratch[:, 1, :], scratch[:, 0, :]))
                        for t in range(TILES):
                            rec = scratch[:, 1, t * LH:(t + 1) * LH].unsqueeze(2).to_broadcast([P, LH, LD])
                            last_ = nc.vector.tensor_tensor(o1[:, t, :].rearrange("p (h e) -> p h e", h=LH),
                                                            nd4[:, t, :, 0:LD], rec, ALU.mult)
                        last_.then_inc(o1_ready, 1)

                r["merged"] = lambda pair: mm.full(unit[("merge", l, pair)])
                att.vector(dve, it, r, lambda seq, pair, hh, i: nrq[:, 2 * seq + i, 2 * pair + hh:2 * pair + hh + 1],
                           l * LAYER_UNITS, linear_terms if l == 0 else None)
                xc = xn if l == 0 else xb
                dve.wait_ge(mm_done, mm.done(unit[("wo", l)]))
                nc.vector.tensor_tensor(h[:, :, 0:HD], xc[:, :, 0:HD], y[:, :, 0:HD], ALU.add)
                nc.vector.tensor_tensor(xa[:, :, :], xc[:, :, :], y[:, :, :], ALU.add).then_inc(x2_ready, 1)
                dve.wait_ge(x2_ready, it * LAYERS + (l + 1))
                dve.wait_ge(mm_done, mm.done(unit[("shift", l)]))
                layernorm(nc, c, link, lambda t: h[:, t, :], lambda t: h[:, t, :], stats, mv, rstd, scratch)\
                    .then_inc(hn_ready, 1)
                if l + 1 == LAYERS:
                    layernorm(nc, c, link, lambda t: xn[:, t, :], lambda t: xt(TILES + t), stats, mv, rstd, scratch)\
                        .then_inc(xn_ready, 1)
                for i, (f0, rows) in enumerate(GCHUNKS):
                    kk = r["s"].take()
                    dve.wait_ge(mm_done, mm.done(unit[("g", l, i)]))
                    dve.wait_ge(s_full, r["s"].full(kk))
                    nc.vector.scalar_tensor_tensor(out=glu[0:rows, i, :], in0=m.s_ps[kk % 2][0:rows, :],
                                                   scalar=gb1[0:rows, l, 0, i:i + 1], in1=gl[0:rows, i, :],
                                                   op0=ALU.add, op1=ALU.mult).then_inc(s_done, 1)
                dve.wait_ge(mm_done, mm.done(unit[("down", l)]))
                link(nc.vector.tensor_tensor(y[:, :, :], y[:, :, :], gb2[:, l, :].unsqueeze(1).to_broadcast([P, TILES, P]), ALU.add))
                nc.vector.tensor_tensor(xb[:, :, :], xa[:, :, :], y[:, :, :], ALU.add).then_inc(x3_ready, 1)
                dve.wait_ge(x3_ready, it * LAYERS + (l + 1))
            s4 = s1[:, :].rearrange("p (t d) -> p t d", t=TILES)
            link(nc.vector.tensor_tensor(s4, s4, lbo[:, :].unsqueeze(1).to_broadcast([P, TILES, P]), ALU.add))
            dve.wait_ge(th_ready, it + 1)
            link(nc.vector.scalar_tensor_tensor(out=f_th[:, :, :], in0=f_th[:, :, :], scalar=1.0, in1=xb[:, :, :],
                                                op0=ALU.add, op1=ALU.mult))
            link(nc.vector.tensor_tensor(f_th[:, :, :], f_th[:, :, :], s4, ALU.mult))
            for t in range(TILES):
                last = nc.vector.scalar_tensor_tensor(out=xt(t), in0=f_th[:, t, :], scalar=0.5, in1=xt(t),
                                                      op0=ALU.mult, op1=ALU.add)
            last.then_inc(out_ready, 1)
            link.close()


def program(nc, c, w, x_in, x_out):
    def body(ctx):
        def sb(name, shape):
            return ctx.enter_context(nc.sbuf_tensor(name, shape, FP32))

        x_all = sb("x_all", [P, NSEQ * SEQ // P + TILES, P])
        c1 = pass1_operands(nc, ctx)
        c.ident = sb("ident", [P, P])
        c.mask0 = sb("mask0", [P, SB])
        c.mask1 = sb("mask1", [P, SB])
        c.sel = sb("sel", [EXPERTS, EXPERTS, P])
        c.rank = sb("rank", [P, EXPERTS])
        c.ps = [ctx.enter_context(nc.psum_tensor(f"ps{i}", [P, 512], FP32)) for i in range(8)]
        c.x_loaded = ctx.enter_context(nc.semaphore("x_loaded"))
        c.const_loaded = ctx.enter_context(nc.semaphore("const_loaded"))
        c.settled = ctx.enter_context(nc.semaphore("settled"))
        c.settled_pool = ctx.enter_context(nc.semaphore("settled_pool"))
        c.stored = ctx.enter_context(nc.semaphore("stored"))
        c.X_LOADS = 4
        c.CONST_LOADS = 16 * 5
        with nc.Block() as block:
            @block.vector
            def _(dve):
                dve.memset(x_all[:, NSEQ * SEQ // P:, :], 0.0).then_inc(c.settled, 1)
                dve.wait_ge(c.settled, 1)

            @block.sync
            def _(sp):
                xi = x_in.rearrange("n (t p) d -> p (n t) d", p=P)
                for i in range(c.X_LOADS):
                    sp.dma_start(x_all[:, 8 * i:8 * i + 8, :], xi[:, 8 * i:8 * i + 8, :]).then_inc(c.x_loaded, 16)
                sp.dma_start(c.ident[:, :], w["c_ident"]).then_inc(c.const_loaded, 16)
                sp.dma_start(c.mask0[:, :], w["c_mask0"]).then_inc(c.const_loaded, 16)
                sp.dma_start(c.mask1[:, :], w["c_mask1"]).then_inc(c.const_loaded, 16)
                sp.dma_start(c.sel[:, :, :], w["c_sel"]).then_inc(c.const_loaded, 16)
                sp.dma_start(c.rank[:, :], w["c_rank"]).then_inc(c.const_loaded, 16)
        with ExitStack() as inner:
            pass0(nc, inner, c, w, c1, x_all)
        with ExitStack() as inner:
            pass1(nc, inner, c, c1, x_all, x_out)

    with ExitStack() as ctx:
        body(ctx)


_INS = {
    "L0_attn_x": "x", "L0_attn_Wq": "Wq", "L0_attn_Wk": "Wk", "L0_attn_Wv": "Wv", "L0_attn_Wo": "Wo",
    "L0_attn_bo": "bo0", "L0_ffn_router_DE": "router", "L0_ffn_w1_eDF": "w1", "L0_ffn_w3_eDF": "w3",
    "L0_ffn_w2_eFD": "w2", "L0_ffn_ws1_DF": "ws1", "L0_ffn_ws3_DF": "ws3", "L0_ffn_ws2_FD": "ws2",
    "L1_attn_Wq": "lWq", "L1_attn_bq": "lbq", "L1_attn_Wk": "lWk", "L1_attn_bk": "lbk", "L1_attn_Wv": "lWv",
    "L1_attn_bv": "lbv", "L1_attn_Wo": "lWo", "L1_attn_bo": "lbo", "L1_ffn_wqkv": "wqkv",
    "L1_ffn_q_scale": "qs", "L1_ffn_k_scale": "ks", "L1_ffn_wo": "fwo", "L1_ffn_ln_g": "lng",
    "L1_ffn_ln_b": "lnb", "L1_ffn_w1": "g1", "L1_ffn_b1": "gb1", "L1_ffn_w2": "g2", "L1_ffn_b2": "gb2",
}
_TRANSPOSED = ("lWq", "lWk", "lWv", "lWo")


def constants():
    import numpy as np
    out = {"c_ident": np.eye(P, dtype=np.float32)}
    i, j = np.arange(P)[:, None], np.arange(P)[None, :]
    far = np.float32(-1e25)
    causal = np.where(j <= i, 0, far).astype(np.float32)
    out["c_mask0"] = np.concatenate([causal, np.zeros((P, P), np.float32), causal], 1)
    near = np.where((j <= i) & (i <= j + HD), 0, far).astype(np.float32)
    before = np.where(i + P <= j + HD, 0, far).astype(np.float32)
    out["c_mask1"] = np.concatenate([near, before, near], 1)
    sel = np.zeros((EXPERTS, EXPERTS, P), np.float32)
    for e in range(EXPERTS):
        sel[e, e] = 1
    out["c_sel"] = sel
    out["c_rank"] = np.tile(np.arange(EXPERTS, 0, -1, dtype=np.float32), (P, 1))
    out["c_tri"] = np.stack([(i <= j), np.ones((P, P)), (i + 1 == j), (i == P - 1) & (j == 0)], 1).astype(np.float32)
    half = np.arange(0, HD, 2, dtype=np.float32)
    inv = (1.0 / np.float32(10000.0) ** (half / np.float32(HD))).astype(np.float32)
    t = np.arange(SEQ, dtype=np.float32)
    fr = t[:, None] * inv[None, :]
    fr = np.concatenate([fr, fr], 1)
    base = ((half + np.float32(0.4 * HD)) / np.float32(1.4 * HD)).astype(np.float32)
    sc = base[None, :] ** ((t - SEQ // 2) / np.float32(HD // 2))[:, None]
    sc = np.concatenate([sc, sc], 1)
    sign = np.concatenate([-np.ones(HD // 2), np.ones(HD // 2)]).astype(np.float32)
    rot = np.stack([np.stack([np.cos(fr) * sc, np.cos(fr) / sc], 1),
                    np.stack([np.sin(fr) * sc * sign, np.sin(fr) / sc * sign], 1)], 1).astype(np.float32)
    out["c_rot"] = np.ascontiguousarray(rot.reshape(2, P, 2, 2, HD).transpose(1, 0, 2, 3, 4))
    return out


def kernel(**inputs):
    import numpy as np
    import concourse.bacc as bacc
    from concourse.bass_utils import run_bass_kernel_spmd

    nc = bacc.Bacc("TRN2", target_bir_lowering=False, num_devices=1)
    arrays, w = {}, {}
    for name, short in _INS.items():
        a = np.asarray(inputs[name])
        a = np.ascontiguousarray(a.T if short in _TRANSPOSED else a)
        arrays[f"in_{short}"] = a
    for name, a in constants().items():
        arrays[f"in_{name}"] = a
    for name, a in arrays.items():
        w[name[3:]] = nc.dram_tensor(name, a.shape, mybir.dt.from_np(a.dtype), kind="ExternalInput").ap()
    out = nc.dram_tensor("out_x", (NSEQ, SEQ, P), FP32, kind="ExternalOutput").ap()
    x = w.pop("x")
    program(nc, Common(), w, x, out)
    r = run_bass_kernel_spmd(nc, [arrays], core_ids=[0])
    return r.results[0]["out_x"]
```
